# Optimizing a Trainium2 kernel written in Bass

```python
import numpy as np
import jax
import jax.numpy as jnp

def _softmax(x, axis=-1):
    return jax.nn.softmax(x, axis=axis)

def _gelu(x):
    return jax.nn.gelu(x, approximate=True)

def _silu(x):
    return jax.nn.silu(x)

def _sigmoid(x):
    return jax.nn.sigmoid(x)

def _layernorm(x, axis=-1, eps=1e-05):
    m = jnp.mean(x, axis=axis, keepdims=True)
    v = jnp.var(x, axis=axis, keepdims=True)
    return (x - m) / jnp.sqrt(v + eps)

def _scatter_add(tgt, idx, src, axis=0):
    return tgt.at[idx].add(src)

def _segment_sum(src, seg, n):
    return jax.ops.segment_sum(src, seg, n)
kernel_name = 'mk_gnn_preln_d4_gnn_r8_5c3e33'

def setup_inputs(seed: int=0):
    np.random.seed(seed)
    _w = jnp.asarray

    def _rec_inputs():
        import jax
        import jax.numpy as jnp
        _gk = jax.random.key(seed)
        x = -0.0005121 + 1.001 * jax.random.normal(jax.random.fold_in(_gk, 1), (12500, 64), jnp.float32)
        _s = jax.random.randint(jax.random.fold_in(_gk, 2), (100000,), 0, 12500, jnp.int32)
        _d = jax.random.randint(jax.random.fold_in(_gk, 3), (100000,), 0, 12500, jnp.int32)
        _loop = jnp.arange(12500, dtype=jnp.int32)
        src = jnp.concatenate([_s, _d, _loop])
        dst = jnp.concatenate([_d, _s, _loop])
        _o = jnp.argsort(dst, stable=True)
        src = src[_o]
        dst = dst[_o]
        edge_type_65 = jax.random.randint(jax.random.fold_in(_gk, 12), (212500,), 0, 65, jnp.int32)
        edge_weight = jax.random.uniform(jax.random.fold_in(_gk, 13), (212500,), jnp.float32, 0.0, 0.999999)
        edge_weight_n2 = jax.random.uniform(jax.random.fold_in(_gk, 14), (212500,), jnp.float32, 0.0, 0.999999)
        return (x, src, dst, edge_type_65, edge_weight, edge_weight_n2)
    x, src, dst, edge_type_65, edge_weight, edge_weight_n2 = _rec_inputs()

    def _L0_gnn_setup():
        import jax, jax.numpy as jnp
        import numpy as np
        N, E, D, R, L = (6250, 75000, 64, 65, 2)

        def _rgcn_conv(x, src, dst, edge_type, W_r, W_root, b):
            n, d = x.shape
            r = W_r.shape[0]
            seg = dst * r + edge_type
            msg = x[src]
            agg = jax.ops.segment_sum(msg, seg, num_segments=n * r).reshape(n, r, d)
            cnt = jax.ops.segment_sum(jnp.ones((msg.shape[0],), x.dtype), seg, num_segments=n * r).reshape(n, r, 1)
            mean = agg / jnp.maximum(cnt, 1.0)
            out = jnp.einsum('nrd,rdk->nk', mean, W_r)
            return out + x @ W_root + b
        key = jax.random.key(seed)
        ks = jax.random.split(key, 10)
        x = jax.random.normal(ks[0], (N, D), dtype=jnp.float32)
        edge_index = jax.random.randint(ks[1], (2, E), 0, N, dtype=jnp.int64)
        edge_type = jax.random.randint(ks[2], (E,), 0, R, dtype=jnp.int64)
        s = 1.0 / np.sqrt(D)
        W = jax.random.normal(ks[3], (L, R, D, D), dtype=jnp.float32) * s
        root = jax.random.normal(ks[4], (L, D, D), dtype=jnp.float32) * s
        bias = jax.random.normal(ks[5], (L, D), dtype=jnp.float32) * 0.01
        res_W = jax.random.normal(ks[6], (L, D, D), dtype=jnp.float32) * s
        res_b = jax.random.normal(ks[7], (L, D), dtype=jnp.float32) * 0.01
        return {'x': x, 'edge_index': edge_index, 'edge_type': edge_type, 'W': W, 'root': root, 'bias': bias, 'res_W': res_W, 'res_b': res_b}
    _L0_gnn_all = _L0_gnn_setup()
    _L0_gnn_in = {k: v for k, v in _L0_gnn_all.items() if k in ('W', 'root', 'bias', 'res_W', 'res_b')}
    del _L0_gnn_all

    def _L1_gnn_setup():
        import jax, jax.numpy as jnp
        import numpy as np
        N, E, D_IN, D_OUT = (8192, 131072, 64, 64)
        EPS = 1e-08
        key = jax.random.key(seed)
        ks = jax.random.split(key, 8)
        h = jax.random.normal(ks[0], (N, D_IN), dtype=jnp.float32)
        edge_index = jax.random.randint(ks[1], (2, E), 0, N, dtype=jnp.int64 if jax.config.jax_enable_x64 else jnp.int32)
        adj_v = jax.random.uniform(ks[2], (E,), dtype=jnp.float32)
        deg_v = jax.random.uniform(ks[3], (E,), dtype=jnp.float32)
        W = jax.random.normal(ks[4], (D_IN, D_OUT), dtype=jnp.float32) / np.sqrt(D_IN)
        b = jax.random.normal(ks[5], (D_OUT,), dtype=jnp.float32) * 0.01
        deg_coeff = jnp.array([0.5, 0.0], dtype=jnp.float32)
        coeff_param = jnp.zeros((3,), dtype=jnp.float32)
        scale_param = 2.0 * jnp.ones((1,), dtype=jnp.float32)
        return {'h': h, 'edge_index': edge_index, 'adj_v': adj_v, 'deg_v': deg_v, 'W': W, 'b': b, 'deg_coeff': deg_coeff, 'coeff_param': coeff_param, 'scale_param': scale_param}
    _L1_gnn_all = _L1_gnn_setup()
    _L1_gnn_in = {k: v for k, v in _L1_gnn_all.items() if k in ('W', 'b', 'deg_coeff', 'coeff_param', 'scale_param')}
    del _L1_gnn_all

    def _L2_gnn_setup():
        import jax, jax.numpy as jnp
        import numpy as np
        N_NODES = 12500
        D_FEAT = 64
        AVG_DEG = 16
        ALPHA = 0.2
        key = jax.random.key(seed)
        k1, k2, k3 = jax.random.split(key, 3)
        N, D, E = (N_NODES, D_FEAT, N_NODES * AVG_DEG)
        inputs = jax.random.normal(k1, (N, D), dtype=jnp.float32)
        src = jnp.repeat(jnp.arange(N, dtype=jnp.int32), AVG_DEG)
        dst = jax.random.randint(k2, (E,), 0, N, dtype=jnp.int32)
        edge_index = jnp.stack([src, dst], axis=0)
        W = jnp.ones((D,), dtype=jnp.float32)
        stdv = 1.0 / np.sqrt(2.0 * D)
        a = jax.random.uniform(k3, (2 * D,), dtype=jnp.float32, minval=-stdv, maxval=stdv)
        return {'inputs': inputs, 'W': W, 'a': a, 'edge_index': edge_index}
    _L2_gnn_all = _L2_gnn_setup()
    _L2_gnn_in = {k: v for k, v in _L2_gnn_all.items() if k in ('W', 'a')}
    del _L2_gnn_all

    def _L3_gnn_setup():
        import jax, jax.numpy as jnp
        import numpy as np
        N_NODES = 12500

        def _gcn_norm(edge_index, num_nodes):
            row, col = (edge_index[0], edge_index[1])
            ones = jnp.ones(edge_index.shape[1], dtype=jnp.float32)
            deg = jax.ops.segment_sum(ones, col, num_segments=num_nodes)
            deg_inv_sqrt = jnp.where(deg > 0, jax.lax.rsqrt(deg), 0.0)
            return deg_inv_sqrt[row] * deg_inv_sqrt[col]

        def _propagate(x, edge_index, norm, num_nodes):
            row, col = (edge_index[0], edge_index[1])
            msgs = norm[:, None] * x[row]
            return jax.ops.segment_sum(msgs, col, num_segments=num_nodes)
        key = jax.random.key(seed)
        k1, k2, k3, k4, k5 = jax.random.split(key, 5)
        node_emb = jax.random.normal(k1, (N_NODES, 64), dtype=jnp.float32)
        edge_index = jax.random.randint(k2, (2, 125000), 0, N_NODES, dtype=jnp.int64)
        W = jax.random.normal(k3, (64, 64), dtype=jnp.float32) * (1.0 / np.sqrt(64.0))
        b = jax.random.normal(k4, (64,), dtype=jnp.float32) * 0.01
        return {'node_emb': node_emb, 'edge_index': edge_index, 'W': W, 'b': b}
    _L3_gnn_all = _L3_gnn_setup()
    _L3_gnn_in = {k: v for k, v in _L3_gnn_all.items() if k in ('W', 'b')}
    del _L3_gnn_all
    return {'x': x, 'src': src, 'dst': dst, 'edge_type_65': edge_type_65, 'edge_weight': edge_weight, 'edge_weight_n2': edge_weight_n2, 'L0_gnn_W': _L0_gnn_in['W'], 'L0_gnn_root': _L0_gnn_in['root'], 'L0_gnn_bias': _L0_gnn_in['bias'], 'L0_gnn_res_W': _L0_gnn_in['res_W'], 'L0_gnn_res_b': _L0_gnn_in['res_b'], 'L1_gnn_W': _L1_gnn_in['W'], 'L1_gnn_b': _L1_gnn_in['b'], 'L1_gnn_deg_coeff': _L1_gnn_in['deg_coeff'], 'L1_gnn_coeff_param': _L1_gnn_in['coeff_param'], 'L1_gnn_scale_param': _L1_gnn_in['scale_param'], 'L2_gnn_W': _L2_gnn_in['W'], 'L2_gnn_a': _L2_gnn_in['a'], 'L3_gnn_W': _L3_gnn_in['W'], 'L3_gnn_b': _L3_gnn_in['b']}

def reference(x, src, dst, edge_type_65, edge_weight, edge_weight_n2, L0_gnn_W, L0_gnn_root, L0_gnn_bias, L0_gnn_res_W, L0_gnn_res_b, L1_gnn_W, L1_gnn_b, L1_gnn_deg_coeff, L1_gnn_coeff_param, L1_gnn_scale_param, L2_gnn_W, L2_gnn_a, L3_gnn_W, L3_gnn_b):
    import jax
    import jax.numpy as jnp

    def _L0_gnn_ref(x, edge_index, edge_type, W, root, bias, res_W, res_b):
        import jax, jax.numpy as jnp
        import numpy as np
        N, E, D, R, L = (6250, 75000, 64, 65, 2)

        def _rgcn_conv(x, src, dst, edge_type, W_r, W_root, b):
            n, d = x.shape
            r = W_r.shape[0]
            seg = dst * r + edge_type
            msg = x[src]
            agg = jax.ops.segment_sum(msg, seg, num_segments=n * r).reshape(n, r, d)
            cnt = jax.ops.segment_sum(jnp.ones((msg.shape[0],), x.dtype), seg, num_segments=n * r).reshape(n, r, 1)
            mean = agg / jnp.maximum(cnt, 1.0)
            out = jnp.einsum('nrd,rdk->nk', mean, W_r)
            return out + x @ W_root + b
        src, dst = (edge_index[0], edge_index[1])
        h = x
        for l in range(W.shape[0]):
            conv = _rgcn_conv(h, src, dst, edge_type, W[l], root[l], bias[l])
            conv = jax.nn.relu(conv)
            res = jax.nn.relu(h @ res_W[l] + res_b[l])
            h = conv + res
        return h

    def _L1_gnn_ref(h, edge_index, adj_v, deg_v, W, b, deg_coeff, coeff_param, scale_param):
        import jax, jax.numpy as jnp
        import numpy as np
        N, E, D_IN, D_OUT = (8192, 131072, 64, 64)
        EPS = 1e-08
        n_nodes = h.shape[0]
        Wh = h @ W + b
        row, col = (edge_index[0], edge_index[1])
        sc = jax.nn.softplus(deg_coeff[0] * deg_v + deg_coeff[1])
        Wr = Wh[row]
        Wc = Wh[col]
        dot = jnp.sum(Wr * Wc, axis=-1)
        nr = jnp.sqrt(jnp.sum(Wr * Wr, axis=-1))
        nc = jnp.sqrt(jnp.sum(Wc * Wc, axis=-1))
        sim = dot / jnp.maximum(nr * nc, EPS)
        sim_pos = jax.nn.relu(sim)
        sim_neg = -jax.nn.relu(-sim)
        no_diag = (row != col).astype(Wh.dtype)
        base = adj_v * sc * no_diag
        prop_pos = jax.ops.segment_sum((base * sim_pos)[:, None] * Wc, row, num_segments=n_nodes)
        prop_neg = jax.ops.segment_sum((base * sim_neg)[:, None] * Wc, row, num_segments=n_nodes)
        coeff = jax.nn.softmax(coeff_param)
        scale = jax.nn.softplus(scale_param)
        return scale * (coeff[0] * prop_pos + coeff[1] * prop_neg + coeff[2] * Wh)

    def _L2_gnn_ref(inputs, W, a, edge_index):
        import jax, jax.numpy as jnp
        import numpy as np
        N_NODES = 12500
        D_FEAT = 64
        AVG_DEG = 16
        ALPHA = 0.2
        N, D = inputs.shape
        src, dst = (edge_index[0], edge_index[1])
        h = inputs * W
        s_src = h @ a[:D]
        s_dst = h @ a[D:]
        score = s_src[src] + s_dst[dst]
        edge_e = jnp.exp(jax.nn.leaky_relu(score, negative_slope=ALPHA))
        e_rowsum = jax.ops.segment_sum(edge_e, src, num_segments=N)
        h_prime = jax.ops.segment_sum(edge_e[:, None] * h[dst], src, num_segments=N)
        h_prime = h_prime / e_rowsum[:, None]
        return jax.nn.elu(h_prime)

    def _L3_gnn_ref(node_emb, edge_index, W, b):
        import jax, jax.numpy as jnp
        import numpy as np
        N_NODES = 12500

        def _gcn_norm(edge_index, num_nodes):
            row, col = (edge_index[0], edge_index[1])
            ones = jnp.ones(edge_index.shape[1], dtype=jnp.float32)
            deg = jax.ops.segment_sum(ones, col, num_segments=num_nodes)
            deg_inv_sqrt = jnp.where(deg > 0, jax.lax.rsqrt(deg), 0.0)
            return deg_inv_sqrt[row] * deg_inv_sqrt[col]

        def _propagate(x, edge_index, norm, num_nodes):
            row, col = (edge_index[0], edge_index[1])
            msgs = norm[:, None] * x[row]
            return jax.ops.segment_sum(msgs, col, num_segments=num_nodes)
        num_nodes = node_emb.shape[0]
        norm = _gcn_norm(edge_index, num_nodes)
        h1 = _propagate(node_emb, edge_index, norm, num_nodes)
        h2 = _propagate(h1, edge_index, norm, num_nodes)
        combined = (node_emb + h1 + h2) * 0.3
        return combined @ W.T + b
    edge_index = jnp.stack([src, dst])
    h = jnp.maximum(_layernorm(x, axis=-1), 0.0)
    x = x + _L0_gnn_ref(h, edge_index, edge_type_65, L0_gnn_W, L0_gnn_root, L0_gnn_bias, L0_gnn_res_W, L0_gnn_res_b)
    h = jnp.maximum(_layernorm(x, axis=-1), 0.0)
    x = x + _L1_gnn_ref(h, edge_index, edge_weight, edge_weight_n2, L1_gnn_W, L1_gnn_b, L1_gnn_deg_coeff, L1_gnn_coeff_param, L1_gnn_scale_param)
    h = jnp.maximum(_layernorm(x, axis=-1), 0.0)
    x = x + _L2_gnn_ref(h, L2_gnn_W, L2_gnn_a, edge_index)
    h = jnp.maximum(_layernorm(x, axis=-1), 0.0)
    x = x + _L3_gnn_ref(h, edge_index, L3_gnn_W, L3_gnn_b)
    return x

_drawn_inputs = setup_inputs


def setup_inputs(seed=0):
    import zlib

    import numpy as np

    out = dict(_drawn_inputs(seed))
    spreads = {'L1_gnn_coeff_param': (0.0, 0.8), 'L2_gnn_W': (1.0, 0.6)}
    factors = {'edge_weight_n2': 8.0,
     'L0_gnn_bias': 8.0,
     'L0_gnn_res_b': 8.0,
     'L1_gnn_b': 8.0,
     'L1_gnn_deg_coeff': 4.737,
     'L2_gnn_a': 8.0,
     'L3_gnn_b': 42.961}
    for name, (base, spread) in spreads.items():
        noise = np.random.default_rng([zlib.crc32(name.encode()), seed]).standard_normal(out[name].shape)
        drawn = base * np.exp(spread * noise) if base else spread * noise
        out[name] = jnp.asarray(drawn.astype(out[name].dtype))
    for name, factor in factors.items():
        out[name] = (out[name] * factor).astype(out[name].dtype)
    return out
```

```python
from contextlib import ExitStack

import concourse.bass as bass
from concourse import mybir

ALU = mybir.AluOpType
ACT = mybir.ActivationFunctionType
AX = mybir.AxisListType
F32 = mybir.dt.float32
BF16 = mybir.dt.bfloat16
I32 = mybir.dt.int32
U16 = mybir.dt.uint16
ENG = mybir.EngineType

P = 128
D = 64
N = 12500
NB = -(-N // P)
NLAST = N - (NB - 1) * P
E = 212500
EP = 125
EC = E // EP
R = 65
G = 8
NG = -(-((E + NB * (P - 1)) // P) // (2 * G)) * 2
TT = NG * G
WIDE = D + 4
SC = 10
LN_EPS = 1e-5


class Count:

    def __init__(self):
        self.now = 0

    def up(self, by=1):
        self.now += by
        return by


def cast_rows(ap, n):
    return ap.broadcast_to([n, ap.shape[1]])


class Signals:

    def __init__(self):
        self.nc, self.held = None, []

    def start(self, nc):
        self.nc, self.held = nc, []

    def new(self, name):
        self.held.append(self.nc.alloc_semaphore(name))
        return self.held[-1]

    def clear(self):
        self.nc.clear_and_free_semaphores(self.held)
        self.nc.all_engine_barrier()
        self.held = []


signals = Signals()


class Step:

    def __init__(self, g, slot, half):
        self.g, self.slot, self.half = g, slot, half

    def next(self):
        return Step(self.g + 1, 1 - self.slot, self.half + self.slot)

    def next2(self):
        return Step(self.g + 2, self.slot, self.half + 1)

    def before(self):
        return Step(self.g - 1, 1 - self.slot, self.half - (1 - self.slot))

    def first(self):
        return isinstance(self.g, int) and self.g == 0

    def last(self, n, count):
        return isinstance(self.g, int) and self.g + n >= count


def over_steps(eng, count, body):
    assert count % 2 == 0
    body(Step(0, 0, 0))
    body(Step(1, 1, 0))
    with eng.Fori(1, count // 2 - 1) as i:
        body(Step(i * 2, 0, i))
        body(Step(i * 2 + 1, 1, i))
    body(Step(count - 2, 0, count // 2 - 1))
    body(Step(count - 1, 1, count // 2 - 1))


def wait_positive(eng, sem, value):
    if isinstance(value, int) and value <= 0:
        return
    eng.wait_ge(sem, value)


def load_blocks(nc, engine, row, g, width=WIDE):
    _, values = nc.values_load_multi_w_load_instructions(
        row[:, bass.ds(g * G, G)], engines=[engine], min_val=0, max_val=(NB - 1) * width,
        skip_runtime_bounds_check_because="the row is clipped to the last block when it is made")
    return values


def edge_pass(nc, name, kind, c, rec, f_index, f_local, acc, aw, table=None, tw=0,
              own=None, ow=0, own_row=None, acc_row=None, beside=None):
    gathers = kind != "count"
    looks = kind in ("typed", "cosine", "attention")
    typed = kind in ("typed", "count")
    weighs = kind not in ("plain", "count")
    mdt = BF16 if kind == "count" else F32
    KW = {"typed": 4, "typed_again": 1, "cosine": 10, "attention": 3}.get(kind, 0)
    banks = 1 if G * aw <= 512 else 2
    per = G // banks
    with ExitStack() as ctx:
        def sb(n, shape, dt=F32):
            return ctx.enter_context(nc.sbuf_tensor(f"{name}_{n}", shape, dt))

        def ps(n, shape):
            return ctx.enter_context(nc.psum_tensor(f"{name}_{n}", shape, F32))

        def sem(n):
            return signals.new(f"{name}_{n}")

        mask = [sb(f"mask{s}", [P, G, P], mdt) for s in range(2)]
        sums = [ps(f"sums{s}", [P, banks, 512]) for s in range(2)]
        if gathers:
            index = [sb(f"index{s}", [P, G], I32) for s in range(2)]
            rows = [sb(f"rows{s}", [P, G, tw]) for s in range(2)]
        if weighs:
            msg = [sb(f"msg{s}", [P, G, aw]) for s in range(2)]
        if looks:
            mask_t = sb("mask_t", [P, G, P])
            turned = ps("turned", [P, G, P])
            found = ps("found", [P, 2, 512])
            prod = sb("prod", [P, G, R])
            small = sb("small", [P, 8, G])
        if typed:
            kinds = [sb(f"kinds{s}", [P, G, R], mdt) for s in range(2)]

        cleared = sem("cleared")
        masked = sem("masked")
        gathered = [sem(f"gathered{s}") for s in range(2)]
        staged = sem("staged")
        stage_turn = sem("stage_turn")
        pool_turn = sem("pool_turn")
        weighed = sem("weighed")
        summed = sem("summed")
        added = sem("added")
        if looks:
            turn = sem("turn")
            turned_out = sem("turned_out")
            found_s = sem("found")
            expd = sem("expd")

        def field(f, g):
            return rec[:, bass.ds(g * G, G), f]

        def sum_ap(slot, j):
            return sums[slot][:, j // per, (j % per) * aw:(j % per) * aw + aw]

        def found_ap(w):
            return found[:, :, 0:(G // 2) * w].rearrange("p h (j w) -> p h j w", w=w)

        with nc.Block() as block:
            if gathers:
                @block.gpsimd
                def _(pool):
                    def step(s):
                        pool.wait_ge(staged, s.g + 1)
                        if kind == "plain":
                            wait_positive(pool, summed, s.g - 1)
                        else:
                            wait_positive(pool, weighed, (s.g - 1) * KW)
                        pool.sem_inc(pool_turn, 1)
                        for j in range(G):
                            pool.indirect_dma_start(
                                rows[s.slot][:, j, :], None, table,
                                bass.IndirectOffsetOnAxis(ap=index[s.slot][:, j:j + 1], axis=0),
                            ).then_inc(gathered[s.slot], 16)
                    over_steps(pool, NG, step)
            else:
                @block.gpsimd
                def _(pool):
                    beside["pool"](pool)

            @block.scalar
            def _(act):
                if beside is not None:
                    beside["act"](act)

                def stage(s):
                    if not s.first() and not (isinstance(s.g, int) and s.g == 1):
                        act.wait_ge(gathered[s.slot], s.half * (16 * G))
                        act.sem_inc(stage_turn, 1)
                    nc.scalar.copy(index[s.slot][:, :], rec[:, bass.ds(s.g * G, G), f_index].bitcast(I32)).then_inc(staged, 1)

                def turn_out(s):
                    for h in range(2):
                        act.wait_ge(turn, s.g * 2 + (h + 1))
                        if h == 0:
                            wait_positive(act, found_s, s.g)
                        nc.scalar.copy(mask_t[:, 4 * h:4 * h + 4, :], turned[:, 4 * h:4 * h + 4, :]).then_inc(turned_out, 1)

                def step(s):
                    if looks and not s.last(1, NG):
                        turn_out(s.next())
                    if kind == "attention":
                        act.wait_ge(weighed, s.g * KW + 2)
                        nc.scalar.activation(small[:, 2, :], small[:, 1, :], ACT.Exp).then_inc(expd, 1)
                    if gathers and not s.last(2, NG):
                        stage(s.next2())

                if gathers:
                    stage(Step(0, 0, 0))
                    stage(Step(1, 1, 0))
                if looks:
                    turn_out(Step(0, 0, 0))
                if gathers or looks:
                    over_steps(act, NG, step)

            @block.tensor
            def _(pe):
                def transposes(s):
                    pe.wait_ge(masked, s.g + 1)
                    for j in range(G):
                        if j % 4 == 0:
                            wait_positive(pe, turned_out, s.g * 2 + (j // 4 - 1))
                        mm = pe.transpose(turned[:, j, :], mask[s.slot][:, j, :], c["ident"][:, :])
                        if j % 4 == 3:
                            mm.then_inc(turn, 1)

                def look_up(s):
                    offsets = load_blocks(nc, ENG.PE, own_row, s.g, 1 if ow == 1 else WIDE)
                    pe.wait_ge(turned_out, s.g * 2 + 2)
                    wait_positive(pe, weighed, s.g * KW)
                    for j in range(G):
                        mm = pe.matmul(found[:, j // 4, (j % 4) * ow:(j % 4) * ow + ow], mask_t[:, j, :],
                                       own[:, bass.ds(offsets[j], ow)], start=(j % 4 == 0), stop=(j % 4 == 3),
                                       skip_group_check=True)
                    mm.then_inc(found_s, 1)

                def sum_up(s):
                    pe.wait_ge(masked, s.g + 1)
                    if weighs:
                        pe.wait_ge(weighed, (s.g + 1) * KW)
                    elif kind == "plain":
                        pe.wait_ge(gathered[s.slot], (s.half + 1) * (16 * G))
                    wait_positive(pe, added, (s.g - 1) * G)
                    for j in range(G):
                        if kind == "count":
                            what = kinds[s.slot][:, j, :]
                        elif kind == "plain":
                            what = rows[s.slot][:, j, 0:aw]
                        else:
                            what = msg[s.slot][:, j, :]
                        mm = pe.matmul(sum_ap(s.slot, j), mask[s.slot][:, j, :], what,
                                       start=(j % per == 0), stop=(j % per == per - 1), skip_group_check=True)
                    mm.then_inc(summed, 1)

                def step(s):
                    if looks and not s.last(1, NG):
                        transposes(s.next())
                    sum_up(s)
                    if looks and not s.last(1, NG):
                        look_up(s.next())

                if looks:
                    transposes(Step(0, 0, 0))
                    look_up(Step(0, 0, 0))
                over_steps(pe, NG, step)

            @block.vector
            def _(dve):
                def make_masks(s):
                    wait_positive(dve, summed, s.g - 1)
                    if typed:
                        t = field(3, s.g).unsqueeze(2).broadcast_to([P, G, R])
                        dve.tensor_tensor(kinds[s.slot][:, :, :], t,
                                          c["iota"][:, 0:R].unsqueeze(1).broadcast_to([P, G, R]), ALU.is_equal)
                    loc = field(f_local, s.g).unsqueeze(2).broadcast_to([P, G, P])
                    dve.tensor_tensor(mask[s.slot][:, :, :], loc,
                                      c["iota"][:, :].unsqueeze(1).broadcast_to([P, G, P]),
                                      ALU.is_equal).then_inc(masked, 1)

                def chain(s, n):
                    dve.wait_ge(weighed, s.g * KW + n)

                def arrived(s):
                    dve.wait_ge(gathered[s.slot], (s.half + 1) * (16 * G))

                def weigh(s):
                    r, m = rows[s.slot], msg[s.slot]
                    if kind == "typed":
                        dve.wait_ge(found_s, s.g + 1)
                        dve.wait_ge(masked, s.g + 1)
                        dve.tensor_tensor(prod[:, 0:G, :].rearrange("p (h j) w -> p h j w", h=2), found_ap(R),
                                          kinds[s.slot][:, :, :].rearrange("p (h j) w -> p h j w", h=2),
                                          ALU.mult).then_inc(weighed, 1)
                        chain(s, 1)
                        dve.tensor_reduce(small[:, 0, :], prod[:, :, :], AX.X, ALU.add).then_inc(weighed, 1)
                        chain(s, 2)
                        dve.tensor_scalar(c["kept"][:, bass.ds(s.g * G, G)], small[:, 0, :], 1.0, None, ALU.mult).then_inc(weighed, 1)
                        arrived(s)
                        dve.tensor_tensor(m[:, :, :], r[:, :, 0:D], small[:, 0, :].unsqueeze(2).broadcast_to([P, G, D]),
                                          ALU.mult).then_inc(weighed, 1)
                    if kind == "typed_again":
                        arrived(s)
                        dve.tensor_tensor(m[:, :, :], r[:, :, 0:D],
                                          c["kept"][:, bass.ds(s.g * G, G)].unsqueeze(2).broadcast_to([P, G, D]),
                                          ALU.mult).then_inc(weighed, 1)
                    if kind == "cosine":
                        f = found_ap(R)
                        r4 = r[:, :, :].rearrange("p (h j) w -> p h j w", h=2)
                        dve.wait_ge(found_s, s.g + 1)
                        arrived(s)
                        dve.tensor_tensor(prod[:, :, :].rearrange("p (h j) w -> p h j w", h=2), f, r4[:, :, :, 0:R],
                                          ALU.mult).then_inc(weighed, 1)
                        chain(s, 1)
                        dve.tensor_reduce(small[:, 0, :], prod[:, :, 0:D], AX.X, ALU.add).then_inc(weighed, 1)
                        dve.tensor_scalar(small[:, 1, :], prod[:, :, D], 1e-8, None, ALU.max).then_inc(weighed, 1)
                        chain(s, 3)
                        dve.reciprocal(small[:, 2, :], small[:, 1, :]).then_inc(weighed, 1)
                        chain(s, 4)
                        dve.tensor_tensor(small[:, 3, :], small[:, 0, :], small[:, 2, :], ALU.mult).then_inc(weighed, 1)
                        chain(s, 5)
                        dve.tensor_scalar(small[:, 4, :], small[:, 3, :], 0.0, c["coeff"][:, 0:1], ALU.max, ALU.mult).then_inc(weighed, 1)
                        dve.tensor_scalar(small[:, 5, :], small[:, 3, :], 0.0, c["coeff"][:, 1:2], ALU.min, ALU.mult).then_inc(weighed, 1)
                        chain(s, 7)
                        dve.tensor_tensor(small[:, 6, :], small[:, 4, :], small[:, 5, :], ALU.add).then_inc(weighed, 1)
                        chain(s, 8)
                        dve.tensor_tensor(small[:, 7, :], small[:, 6, :], field(2, s.g), ALU.mult).then_inc(weighed, 1)
                        chain(s, 9)
                        dve.tensor_tensor(m[:, :, :], r[:, :, 0:D], small[:, 7, :].unsqueeze(2).broadcast_to([P, G, D]),
                                          ALU.mult).then_inc(weighed, 1)
                    if kind == "attention":
                        dve.wait_ge(found_s, s.g + 1)
                        arrived(s)
                        dve.tensor_tensor(small[:, 0, :].rearrange("p (h j) -> p h j", h=2), found[:, :, 0:G // 2],
                                          r[:, :, D + 1].rearrange("p (h j) -> p h j", h=2), ALU.add).then_inc(weighed, 1)
                        chain(s, 1)
                        dve.scalar_tensor_tensor(out=small[:, 1, :], in0=small[:, 0, :], scalar=0.2, in1=small[:, 0, :],
                                                 op0=ALU.mult, op1=ALU.max).then_inc(weighed, 1)

                def weigh_attention(s):
                    dve.wait_ge(expd, s.g + 1)
                    dve.tensor_tensor(msg[s.slot][:, :, :], rows[s.slot][:, :, 0:aw],
                                      small[:, 2, :].unsqueeze(2).broadcast_to([P, G, aw]), ALU.mult).then_inc(weighed, 1)

                def add_sums(s):
                    offsets = load_blocks(nc, ENG.DVE, acc_row, s.g)
                    dve.wait_ge(summed, s.g + 1)
                    for j in range(G):
                        wait_positive(dve, added, s.g * G + j)
                        to = acc[:, bass.ds(offsets[j], aw)]
                        dve.tensor_tensor(to, to, sum_ap(s.slot, j), ALU.add).then_inc(added, 1)

                def step(s):
                    if not s.last(1, NG):
                        make_masks(s.next())
                    if weighs:
                        weigh(s)
                    if not s.first():
                        add_sums(s.before())
                    if kind == "attention":
                        weigh_attention(s)

                dve.memset(acc[:, :], 0.0).then_inc(cleared, 1)
                dve.wait_ge(cleared, 1)
                make_masks(Step(0, 0, 0))
                over_steps(dve, NG, step)
                add_sums(Step(NG - 1, 1, NG // 2 - 1))


def normalize(nc, name, x, h, tmp):
    with ExitStack() as ctx:
        stat = ctx.enter_context(nc.sbuf_tensor(f"{name}_stat", [P, 3, NB], F32))
        done = signals.new(f"{name}_done")
        rooted = signals.new(f"{name}_rooted")
        x3, h3, t3 = x, h, tmp[:, :, 0:D]

        def spread(i):
            return stat[:, i, :].unsqueeze(2).broadcast_to([P, NB, D])
        with nc.Block() as block:
            @block.scalar
            def _(act):
                act.wait_ge(done, 6)
                nc.scalar.activation(stat[:, 1, :], stat[:, 1, :], ACT.Sqrt).then_inc(rooted, 1)

            @block.vector
            def _(dve):
                dve.tensor_reduce(stat[:, 0, :], x3, AX.X, ALU.add).then_inc(done, 1)
                dve.wait_ge(done, 1)
                dve.tensor_scalar(stat[:, 0, :], stat[:, 0, :], 1.0 / D, None, ALU.mult).then_inc(done, 1)
                dve.wait_ge(done, 2)
                dve.tensor_tensor(h3, x3, spread(0), ALU.subtract).then_inc(done, 1)
                dve.wait_ge(done, 3)
                dve.tensor_tensor(t3, h3, h3, ALU.mult).then_inc(done, 1)
                dve.wait_ge(done, 4)
                dve.tensor_reduce(stat[:, 1, :], t3, AX.X, ALU.add).then_inc(done, 1)
                dve.wait_ge(done, 5)
                dve.tensor_scalar(stat[:, 1, :], stat[:, 1, :], 1.0 / D, LN_EPS, ALU.mult, ALU.add).then_inc(done, 1)
                dve.wait_ge(rooted, 1)
                dve.reciprocal(stat[:, 2, :], stat[:, 1, :]).then_inc(done, 1)
                dve.wait_ge(done, 7)
                dve.tensor_scalar(h3, h3, 0.0, None, ALU.max).then_inc(done, 1)
                dve.wait_ge(done, 8)
                dve.tensor_tensor(h3, h3, spread(2), ALU.mult).then_inc(done, 1)


def times_weights(nc, name, c, h, w2, f, consume, k):
    pairs = NB // 2
    with ExitStack() as ctx:
        pair = [ctx.enter_context(nc.sbuf_tensor(f"{name}_pair{s}", [P, P], F32)) for s in range(2)]
        ht = [ctx.enter_context(nc.sbuf_tensor(f"{name}_ht{s}", [P, P], F32)) for s in range(2)]
        tp = [ctx.enter_context(nc.psum_tensor(f"{name}_tp{s}", [P, 512], F32)) for s in range(2)]
        out = [ctx.enter_context(nc.psum_tensor(f"{name}_out{s}", [P, 2, 512], F32)) for s in range(2)]
        names = ["copied", "turned", "turned_out", "product", "used", "copy_turn"]
        copied, turned, turned_out, product, used, copy_turn = (
            signals.new(f"{name}_{n}") for n in names)

        def over_pairs(eng, body):
            for g in range(3):
                body(Step(g, g % 2, g // 2))
            with eng.Fori(1, pairs // 2) as i:
                body(Step(i * 2 + 1, 1, i))
                body(Step(i * 2 + 2, 0, i + 1))

        with nc.Block() as block:
            @block.scalar
            def _(act):
                def copy_in(s):
                    if not s.first():
                        wait_positive(act, turned, s.g - 1)
                        act.sem_inc(copy_turn, 1)
                    nc.scalar.copy(pair[s.slot][:, :], h[:, bass.ds(s.g * P, P)]).then_inc(copied, 1)

                def step(s):
                    copy_in(s)
                    act.wait_ge(turned, s.g + 1)
                    wait_positive(act, product, s.g - 1)
                    nc.scalar.copy(ht[s.slot][:, :], tp[s.slot][:, 0:P]).then_inc(turned_out, 1)
                over_pairs(act, step)

            @block.tensor
            def _(pe):
                def step(s):
                    pe.wait_ge(copied, s.g + 1)
                    wait_positive(pe, turned_out, s.g - 1)
                    pe.transpose(tp[s.slot][:, 0:P], pair[s.slot][:, :], c["ident"][:, :]).then_inc(turned, 1)
                    pe.wait_ge(turned_out, s.g + 1)
                    wait_positive(pe, used, (s.g - 1) * k)
                    for j in range(2):
                        mm = pe.matmul(out[s.slot][:, j, 0:f], ht[s.slot][D * j:D * j + D, :], w2[D * j:D * j + D, 0:f],
                                       start=True, stop=True)
                    mm.then_inc(product, 1)
                over_pairs(pe, step)

            @block.vector
            def _(dve):
                def step(s):
                    dve.wait_ge(product, s.g + 1)
                    consume(dve, s, out[s.slot][:, :, 0:f], used)
                over_pairs(dve, step)


YC = 4
YW = R * D // (4 * YC)
YQ = YC * YW


def typed_rows(nc, block, ctx, name, c, h, w2, table):
    pairs = NB // 2
    pair = ctx.enter_context(nc.sbuf_tensor(f"{name}_pair", [P, P], F32))
    ht = ctx.enter_context(nc.sbuf_tensor(f"{name}_ht", [P, P], F32))
    buf = [ctx.enter_context(nc.sbuf_tensor(f"{name}_buf{s}", [P, 2, YQ], F32)) for s in range(2)]
    tp = ctx.enter_context(nc.psum_tensor(f"{name}_tp", [P, 512], F32))
    out = [ctx.enter_context(nc.psum_tensor(f"{name}_out{s}", [P, 2, 512], F32)) for s in range(2)]
    names = ["copied", "turned", "turned_out", "product", "taken", "turn"]
    copied, turned, turned_out, product, taken, turn = (
        signals.new(f"{name}_{n}") for n in names)
    stored = [signals.new(f"{name}_stored{s}") for s in range(2)]
    dram = table.rearrange("(b p r) d -> p b (r d)", p=P, r=R)
    C = 4 * YC

    def pe_program(pe, loaded):
        pe.wait_ge(loaded, 32)

        def step(i):
            pe.wait_ge(copied, i + 1)
            pe.transpose(tp[:, 0:P], pair[:, :], c["ident"][:, :]).then_inc(turned, 1)
            pe.wait_ge(turned_out, i + 1)
            for q in range(C):
                wait_positive(pe, taken, i * C + (q - 1))
                for j in range(2):
                    mm = pe.matmul(out[q % 2][:, j, 0:YW], ht[D * j:D * j + D, :],
                                   w2[D * j:D * j + D, q * YW:(q + 1) * YW], start=True, stop=True)
                mm.then_inc(product, 1)
        step(0)
        with pe.Fori(1, pairs) as i:
            step(i)

    def act_program(act):
        def step(i):
            if not isinstance(i, int):
                act.wait_ge(turned, i)
                act.sem_inc(turn, 1)
            nc.scalar.copy(pair[:, :], h[:, bass.ds(i * P, P)]).then_inc(copied, 1)
            act.wait_ge(turned, i + 1)
            wait_positive(act, product, i * C)
            nc.scalar.copy(ht[:, :], tp[:, 0:P]).then_inc(turned_out, 1)
            for q in range(C):
                if q % YC == 0:
                    wait_positive(act, stored[(q // YC) % 2], i * 32 + 16 * (q // (2 * YC)))
                act.wait_ge(product, i * C + (q + 1))
                o = (q % YC) * YW
                nc.scalar.copy(buf[(q // YC) % 2][:, :, o:o + YW], out[q % 2][:, :, 0:YW]).then_inc(taken, 1)
        step(0)
        with act.Fori(1, pairs) as i:
            step(i)

    def sp_program(sp):
        def step(i):
            for u in range(4):
                sp.wait_ge(taken, i * C + (u + 1) * YC)
                sp.dma_start(dram[:, bass.ds(i * 2, 2), u * YQ:(u + 1) * YQ], buf[u % 2][:, :, :]).then_inc(stored[u % 2], 16)
        step(0)
        with sp.Fori(1, pairs) as i:
            step(i)
        for s in range(2):
            sp.wait_ge(stored[s], pairs * 32)

    return pe_program, act_program, sp_program


def typed_weights(nc, ctx, name, w):
    tile = ctx.enter_context(nc.sbuf_tensor(name, [P, R * D], F32))
    loaded = signals.new(f"{name}_loaded")

    def load(sp):
        for half in range(2):
            sp.dma_start(tile[half * D:half * D + D, :].rearrange("k (r o) -> k r o", r=R),
                         w.rearrange("r k o -> k r o")).then_inc(loaded, 16)
    return tile, load, loaded


def store_table(nc, name, tile, table, width):
    with ExitStack() as ctx:
        stored = signals.new(f"{name}_stored")
        with nc.Block() as block:
            @block.sync
            def _(sp):
                for half in range(2):
                    a, b = half * (NB // 2), (half + 1) * (NB // 2)
                    sp.dma_start(table.rearrange("(b p) d -> p b d", p=P)[:, a:b, :], tile[:, a:b, :]).then_inc(stored, 16)
                sp.wait_ge(stored, 32)


def make_records(nc, c, src, dst, etype, ew, ew2, deg_coeff, rec_a, rec_b, key_a, key_b):
    with ExitStack() as ctx:
        def sb(n, shape, dt=F32):
            return ctx.enter_context(nc.sbuf_tensor(f"rec_{n}", shape, dt))

        def sem(n):
            return signals.new(f"rec_{n}")
        s_i, d_i, t_i, n_i = (sb(n, [EP, EC], I32) for n in ("src", "dst", "type", "whole"))
        w1, w2 = sb("w1", [EP, EC]), sb("w2", [EP, EC])
        dc = sb("dc", [P, 2])
        neg = sb("neg", [EP, EC])
        loaded, done, exps = sem("loaded"), sem("done"), sem("exps")
        ra, rb = rec_a[0:EP, 0:EC, :], rec_b[0:EP, 0:EC, :]
        n = Count()
        with nc.Block() as block:
            @block.sync
            def _(sp):
                for to, of in ((s_i, src), (d_i, dst), (t_i, etype), (w1, ew), (w2, ew2)):
                    sp.dma_start(to[:, :], of.rearrange("(p c) -> p c", c=EC)).then_inc(loaded, 16)
                sp.dma_start(dc[:, :], cast_rows(deg_coeff.rearrange("(a d) -> a d", a=1), P)).then_inc(loaded, 16)

            @block.vector
            def _(dve):
                def done_all():
                    dve.wait_ge(done, n.now)
                dve.wait_ge(loaded, 96)
                dve.tensor_scalar(w2[:, :], w2[:, :], dc[0:EP, 0:1], dc[0:EP, 1:2], ALU.mult, ALU.add).then_inc(done, n.up())
                done_all()
                dve.tensor_scalar(neg[:, :], w2[:, :], -1.0, None, ALU.mult).then_inc(done, n.up())
                done_all()
                dve.tensor_tensor(neg[:, :], neg[:, :], w2[:, :], ALU.min).then_inc(done, n.up())
                dve.tensor_copy(ra[:, :, 1].bitcast(I32), s_i[:, :]).then_inc(done, n.up())
                dve.tensor_copy(ra[:, :, 3], t_i[:, :]).then_inc(done, n.up())
                dve.tensor_single_scalar(n_i[:, :], d_i[:, :], P - 1, ALU.bitwise_and).then_inc(done, n.up())
                done_all()
                dve.tensor_copy(ra[:, :, 2], n_i[:, :]).then_inc(done, n.up())
                dve.scalar_tensor_tensor(out=ra[:, :, 0].bitcast(I32), in0=s_i[:, :], scalar=float(R), in1=t_i[:, :],
                                         op0=ALU.mult, op1=ALU.add).then_inc(done, n.up())
                done_all()
                dve.tensor_single_scalar(n_i[:, :], d_i[:, :], 7, ALU.logical_shift_right).then_inc(done, n.up())
                done_all()
                dve.tensor_copy(key_a[:, :], n_i[:, :]).then_inc(done, n.up())
                done_all()
                dve.tensor_single_scalar(n_i[:, :], s_i[:, :], P - 1, ALU.bitwise_and).then_inc(done, n.up())
                done_all()
                dve.tensor_copy(rb[:, :, 1], n_i[:, :]).then_inc(done, n.up())
                dve.tensor_copy(rb[:, :, 0].bitcast(I32), d_i[:, :]).then_inc(done, n.up())
                done_all()
                dve.tensor_single_scalar(n_i[:, :], s_i[:, :], 7, ALU.logical_shift_right).then_inc(done, n.up())
                done_all()
                dve.tensor_copy(key_b[:, :], n_i[:, :]).then_inc(done, n.up())
                dve.tensor_tensor(rb[:, :, 3], s_i[:, :], d_i[:, :], ALU.not_equal).then_inc(done, n.up())
                done_all()
                dve.tensor_tensor(w1[:, :], w1[:, :], rb[:, :, 3], ALU.mult).then_inc(done, n.up())
                done_all()
                dve.wait_ge(exps, 2)
                dve.scalar_tensor_tensor(out=w2[:, :], in0=w2[:, :], scalar=0.0, in1=neg[:, :],
                                         op0=ALU.max, op1=ALU.add).then_inc(done, n.up())
                done_all()
                dve.tensor_tensor(rb[:, :, 2], w1[:, :], w2[:, :], ALU.mult).then_inc(done, n.up())

            @block.scalar
            def _(act):
                act.wait_ge(done, 3)
                nc.scalar.activation(neg[:, :], neg[:, :], ACT.Exp).then_inc(exps, 1)
                act.wait_ge(exps, 1)
                nc.scalar.activation(neg[:, :], neg[:, :], ACT.Ln, bias=1.0).then_inc(exps, 1)


def find_places(nc, dve, order, c, t, key, place, tiles_of, base_ps, m):
    steps, n = m["steps"], m["n"]

    def last():
        wait_positive(dve, steps, n.now)

    last()
    k = n.now
    with dve.Fori(1, NB + 1) as b:
        dve.wait_ge(steps, b + (k - 1)) if k else None
        dve.tensor_scalar(t["is_b"], key, c["iota"][0:EP, bass.ds(b - 1, 1)], None, ALU.is_equal, ALU.add,
                          accum_out=t["count"][:, bass.ds(b - 1, 1)]).then_inc(steps, 1)
    n.up(NB)
    last()
    dve.sem_inc(m["counted"], 1)
    dve.wait_ge(m["prefixed"], order + 1)
    dve.tensor_scalar(t["tiles_i"][:, :], base_ps[:, 1, 0:NB], float(P - 1), None, ALU.add).then_inc(steps, n.up())
    last()
    dve.tensor_single_scalar(t["tiles_i"][:, :], t["tiles_i"][:, :], 7, ALU.logical_shift_right).then_inc(steps, n.up())
    last()
    dve.tensor_copy(t["tiles"][:, :], t["tiles_i"][:, :]).then_inc(steps, n.up())
    last()
    dve.tensor_tensor_scan(t["ends"][:, :], c["ones"][:, 0:NB], t["tiles"][:, :], 0.0, ALU.mult, ALU.add).then_inc(steps, n.up())
    last()
    dve.tensor_tensor(t["base"][:, :], t["ends"][:, :], t["tiles"][:, :], ALU.subtract).then_inc(steps, n.up())
    last()
    dve.tensor_scalar(t["base"][:, :], t["base"][:, :], float(P), -1.0, ALU.mult, ALU.add).then_inc(steps, n.up())
    last()
    dve.tensor_tensor(t["base"][0:EP, :], t["base"][0:EP, :], base_ps[0:EP, 0, 0:NB], ALU.add).then_inc(steps, n.up())
    last()
    dve.memset(place, 0.0).then_inc(steps, n.up())
    k = n.now
    with dve.Fori(0, NB) as b:
        dve.wait_ge(steps, b * 3 + k)
        dve.tensor_scalar(t["is_b"], key, c["iota"][0:EP, bass.ds(b, 1)], None, ALU.is_equal).then_inc(steps, 1)
        dve.wait_ge(steps, b * 3 + (k + 1))
        dve.tensor_tensor_scan(t["rank"], t["ones_e"], t["is_b"], t["base"][0:EP, bass.ds(b, 1)],
                               ALU.mult, ALU.add).then_inc(steps, 1)
        dve.wait_ge(steps, b * 3 + (k + 2))
        dve.sem_inc(m["turn"], 1)
        dve.copy_predicated(place, t["is_b"].bitcast(U16), t["rank"]).then_inc(steps, 1)
    n.up(3 * NB)
    last()
    place_i = place.bitcast(I32)
    dve.tensor_copy(t["whole"], place).then_inc(steps, n.up())
    last()
    dve.tensor_single_scalar(place_i, t["whole"], P - 1, ALU.bitwise_and).then_inc(steps, n.up())
    dve.tensor_single_scalar(t["whole2"], t["whole"], 7, ALU.logical_shift_right).then_inc(steps, n.up())
    last()
    dve.scalar_tensor_tensor(out=place_i, in0=place_i, scalar=float(TT), in1=t["whole2"], op0=ALU.mult, op1=ALU.add).then_inc(steps, n.up())
    dve.tensor_tensor(t["diag"][0:NB, :], t["ends"][0:NB, :], c["ident"][0:NB, 0:NB], ALU.mult).then_inc(steps, n.up())
    last()
    dve.tensor_reduce(t["end_col"][0:NB, :], t["diag"][0:NB, :], AX.X, ALU.add).then_inc(steps, n.up())
    last()
    quarter = TT // 4
    for q in range(4):
        dve.tensor_scalar(t["after"][0:NB, :], t["iota_t"][0:NB, q * quarter:(q + 1) * quarter], t["end_col"][0:NB, :], None,
                          ALU.is_ge).then_inc(m["compared"], 1)
        dve.wait_ge(m["tiled"], 4 * order + q + 1)
        dve.tensor_scalar(tiles_of[:, q * quarter:(q + 1) * quarter], base_ps[:, 0, 0:quarter], float(NB - 1), None,
                          ALU.min).then_inc(steps, n.up())
    last()
    dve.tensor_scalar(tiles_of[32:64, :], tiles_of[32:64, :], float(WIDE), None, ALU.mult).then_inc(steps, n.up())
    last()


def find_places_pe(pe, order, c, t, base_ps, m, between=None):
    pe.wait_ge(m["counted"], order + 1)
    pe.matmul(base_ps[0:EP, 0, 0:NB], c["lower"][0:EP, 0:EP], t["count"][0:EP, :], start=True, stop=True)
    pe.matmul(base_ps[:, 1, 0:NB], c["ones"][0:EP, :], t["count"][0:EP, :], start=True, stop=True).then_inc(m["prefixed"], 1)
    if between is not None:
        between(pe)
    for q in range(4):
        pe.wait_ge(m["compared"], 4 * order + q + 1)
        pe.matmul(base_ps[:, 0, 0:TT // 4], c["ones"][0:NB, :], t["after"][0:NB, :], start=True, stop=True).then_inc(m["tiled"], 1)


def scatter_records(nc, ctx, name, rec, place, table):
    count = EC // SC
    at = [ctx.enter_context(nc.sbuf_tensor(f"{name}_at{s}", [EP, SC], I32)) for s in range(2)]
    what = [ctx.enter_context(nc.sbuf_tensor(f"{name}_what{s}", [EP, SC, 4], F32)) for s in range(2)]
    staged, stage_turn, pool_turn = (signals.new(f"{name}_{n}") for n in ("staged", "stage_turn", "pool_turn"))
    moved = [signals.new(f"{name}_moved{s}") for s in range(2)]

    def act_program(act):
        def step(s):
            if not isinstance(s.g, int) or s.g > 1:
                act.wait_ge(moved[s.slot], s.half * (16 * SC))
                act.sem_inc(stage_turn, 1)
            nc.scalar.copy(at[s.slot][:, :], place[:, bass.ds(s.g * SC, SC)]).then_inc(staged, 1)
            nc.scalar.copy(what[s.slot][:, :, :], rec[0:EP, bass.ds(s.g * SC, SC), :]).then_inc(staged, 1)
        over_steps(act, count, step)

    def pool_program(pool):
        def step(s):
            pool.wait_ge(staged, s.g * 2 + 2)
            pool.sem_inc(pool_turn, 1)
            for j in range(SC):
                pool.indirect_dma_start(table, bass.IndirectOffsetOnAxis(ap=at[s.slot][:, j:j + 1], axis=0),
                                        what[s.slot][:, j, :], None).then_inc(moved[s.slot], 16)
        over_steps(pool, count, step)
        for s in range(2):
            pool.wait_ge(moved[s], count // 2 * 16 * SC)

    return act_program, pool_program


def fill_order(nc, name, table, pad):
    with ExitStack() as ctx:
        filled = signals.new(f"{name}_filled")
        width = pad.shape[1]
        rows = table.rearrange("(p t) f -> p (t f)", p=P)
        with nc.Block() as block:
            @block.sync
            def _(sp):
                for k in range(TT * 4 // width):
                    sp.dma_start(rows[:, k * width:(k + 1) * width], pad[:, :]).then_inc(filled, 16)
                sp.wait_ge(filled, TT * 4 // width * 16)


def load_order(nc, name, table, rec):
    with ExitStack() as ctx:
        loaded = signals.new(f"{name}_loaded")
        with nc.Block() as block:
            @block.sync
            def _(sp):
                sp.dma_start(rec[:, :, :].rearrange("p t f -> p (t f)"),
                             table.rearrange("(p t) f -> p (t f)", p=P)).then_inc(loaded, 16)
                sp.wait_ge(loaded, 16)


def in_a_row(nc, name, ops):
    with ExitStack() as ctx:
        done = signals.new(f"{name}_done")
        with nc.Block() as block:
            @block.vector
            def _(dve):
                for k, (who, op) in enumerate(ops):
                    if who == "v":
                        wait_positive(dve, done, k)
                        op().then_inc(done, 1)

            @block.scalar
            def _(act):
                for k, (who, op) in enumerate(ops):
                    if who == "a":
                        wait_positive(act, done, k)
                        op().then_inc(done, 1)


def gnn_kernel(nc, x, src, dst, edge_type_65, edge_weight, edge_weight_n2, L0_gnn_W, L0_gnn_root, L0_gnn_bias,
               L0_gnn_res_W, L0_gnn_res_b, L1_gnn_W, L1_gnn_b, L1_gnn_deg_coeff, L1_gnn_coeff_param,
               L1_gnn_scale_param, L2_gnn_W, L2_gnn_a, L3_gnn_W, L3_gnn_b, out):
    signals.start(nc)
    v, a = nc.vector, nc.scalar
    typed_table = nc.dram_tensor("typed_table", [NB * P * R, D], F32).ap()
    node_table = nc.dram_tensor("node_table", [NB * P, WIDE], F32).ap()
    order_a = nc.dram_tensor("order_a", [P * TT, 4], F32).ap()
    order_b = nc.dram_tensor("order_b", [P * TT, 4], F32).ap()

    with ExitStack() as ctx:
        def sb(n, shape, dt=F32):
            return ctx.enter_context(nc.sbuf_tensor(n, shape, dt))

        h = sb("h", [P, NB * D])
        rec_a = sb("rec_a", [P, TT, 4])
        rec_b = sb("rec_b", [P, TT, 4])
        acc = sb("acc", [P, NB * WIDE])
        tab = sb("tab", [P, NB * WIDE])
        kept = sb("kept", [P, TT])
        tiles_a = sb("tiles_a", [P, TT], I32)
        tiles_b = sb("tiles_b", [P, TT], I32)
        c = {n: sb(n, [P, P]) for n in ("ident", "iota", "lower", "ones")}
        c["kept"] = kept
        c["coeff"] = coeff = sb("coeff", [P, 8])
        s_src = sb("s_src", [P, NB])
        inv_deg = sb("inv_deg", [P, NB])
        root_res = [sb(f"root_res{l}", [P, 2 * D]) for l in range(2)]
        biases = [sb(f"biases{l}", [P, 2 * D]) for l in range(2)]
        w_cos, w_out = sb("w_cos", [P, D]), sb("w_out", [P, D])
        rows_of = {n: sb(n, [P, k]) for n, k in
                   (("b_cos", D), ("w_att", D), ("a_att", 2 * D), ("b_out", D), ("cp", 3), ("sp", 1))}
        pad_a, pad_b = sb("pad_a", [P, 176]), sb("pad_b", [P, 176])
        acc3 = acc[:, :].rearrange("p (b w) -> p b w", w=WIDE)
        tab3 = tab[:, :].rearrange("p (b w) -> p b w", w=WIDE)
        h3 = h[:, :].rearrange("p (b d) -> p b d", d=D)

        with ExitStack() as inner:
            col = inner.enter_context(nc.sbuf_tensor("col", [P, 1], F32))
            loaded, made, cleared, iotas = (signals.new(n) for n in
                                            ("c_loaded", "c_made", "c_cleared", "c_iotas"))
            with nc.Block() as block:
                @block.gpsimd
                def _(pool):
                    pool.iota(c["iota"][:, :], [[1, P]], base=0, channel_multiplier=0,
                              allow_small_or_imprecise_dtypes=True).then_inc(iotas, 1)
                    pool.iota(col[:, :], [[1, 1]], base=0, channel_multiplier=1,
                              allow_small_or_imprecise_dtypes=True).then_inc(iotas, 1)

                @block.vector
                def _(dve):
                    dve.memset(h[:, (NB - 1) * D:NB * D], 0.0).then_inc(cleared, 1)
                    dve.memset(c["ones"][:, :], 1.0).then_inc(made, 1)
                    dve.memset(pad_a[:, :], 0.0).then_inc(made, 1)
                    dve.memset(pad_b[:, :], 0.0).then_inc(made, 1)
                    dve.wait_ge(made, 3)
                    dve.memset(pad_a[:, :].rearrange("p (t f) -> p t f", f=4)[:, :, 2], -1.0).then_inc(made, 1)
                    dve.memset(pad_b[:, :].rearrange("p (t f) -> p t f", f=4)[:, :, 1], -1.0).then_inc(made, 1)
                    dve.wait_ge(iotas, 2)
                    dve.tensor_scalar(c["ident"][:, :], c["iota"][:, :], col[:, :], None, ALU.is_equal).then_inc(made, 1)
                    dve.tensor_scalar(c["lower"][:, :], c["iota"][:, :], col[:, :], None, ALU.is_gt).then_inc(made, 1)

                @block.sync
                def _(sp):
                    n = Count()

                    def load(to, of):
                        sp.dma_start(to, of).then_inc(loaded, n.up(16))
                    sp.wait_ge(cleared, 1)
                    load(h3[:, 0:NB - 1, :], x[0:(NB - 1) * P, :].rearrange("(b p) d -> p b d", p=P))
                    load(h3[0:NLAST, NB - 1, :], x[(NB - 1) * P:N, :])
                    for half in range(2):
                        at = slice(half * D, half * D + D)
                        for l in range(2):
                            load(root_res[l][at, 0:D], L0_gnn_root[l])
                            load(root_res[l][at, D:2 * D], L0_gnn_res_W[l])
                        load(w_cos[at, :], L1_gnn_W)
                        with nc.allow_non_contiguous_dma(reason="a small transposed weight, once"):
                            load(w_out[at, :], L3_gnn_W.rearrange("o k -> k o"))
                    for l in range(2):
                        load(biases[l][:, 0:D], cast_rows(L0_gnn_bias[l:l + 1, :], P))
                        load(biases[l][:, D:2 * D], cast_rows(L0_gnn_res_b[l:l + 1, :], P))
                    for n_, of in (("b_cos", L1_gnn_b), ("w_att", L2_gnn_W), ("a_att", L2_gnn_a), ("b_out", L3_gnn_b),
                                   ("cp", L1_gnn_coeff_param), ("sp", L1_gnn_scale_param)):
                        load(rows_of[n_][:, :], cast_rows(of.rearrange("(a d) -> a d", a=1), P))
                    sp.wait_ge(loaded, n.now)

        cp, sc = rows_of["cp"], rows_of["sp"]
        in_a_row(nc, "coefficients", [
            ("v", lambda: v.tensor_reduce(coeff[:, 4:5], cp[:, :], AX.X, ALU.max)),
            ("v", lambda: v.tensor_scalar(cp[:, :], cp[:, :], coeff[:, 4:5], None, ALU.subtract)),
            ("a", lambda: a.activation(cp[:, :], cp[:, :], ACT.Exp)),
            ("v", lambda: v.tensor_reduce(coeff[:, 4:5], cp[:, :], AX.X, ALU.add)),
            ("v", lambda: v.reciprocal(coeff[:, 5:6], coeff[:, 4:5])),
            ("v", lambda: v.tensor_scalar(coeff[:, 0:3], cp[:, :], coeff[:, 5:6], None, ALU.mult)),
            ("v", lambda: v.tensor_scalar(coeff[:, 6:7], sc[:, :], -1.0, None, ALU.mult)),
            ("v", lambda: v.tensor_tensor(coeff[:, 6:7], coeff[:, 6:7], sc[:, :], ALU.min)),
            ("a", lambda: a.activation(coeff[:, 7:8], coeff[:, 6:7], ACT.Exp)),
            ("a", lambda: a.activation(coeff[:, 7:8], coeff[:, 7:8], ACT.Ln, bias=1.0)),
            ("v", lambda: v.tensor_scalar(coeff[:, 6:7], sc[:, :], 0.0, None, ALU.max)),
            ("v", lambda: v.tensor_tensor(coeff[:, 3:4], coeff[:, 6:7], coeff[:, 7:8], ALU.add)),
        ])
        normalize(nc, "norm0", h3, h3, acc3)

        accb = acc[0:EP, :].bitcast(BF16)
        key_a, key_b, is_b, ones_e = (accb[:, k * EC:(k + 1) * EC] for k in range(4))
        t = {
            "is_b": is_b, "ones_e": ones_e, "rank": acc[0:EP, 2 * EC:3 * EC],
            "whole": tab[0:EP, 0:EC].bitcast(I32), "whole2": tab[0:EP, EC:2 * EC].bitcast(I32),
            "iota_t": tab[:, 2 * EC:2 * EC + TT],
        }
        place_a = kept[0:EP, 0:EC]
        make_records(nc, c, src, dst, edge_type_65, edge_weight, edge_weight_n2, L1_gnn_deg_coeff, rec_a, rec_b, key_a, key_b)

        with ExitStack() as sort:
            place_b = sort.enter_context(nc.sbuf_tensor("place_b", [EP, EC], F32))[:, :]
            with ExitStack() as inner:
                for n_, shape, dt in (("tiles_i", [P, NB], I32), ("tiles", [P, NB], F32), ("ends", [P, NB], F32),
                                      ("base", [P, NB], F32), ("count", [EP, NB], F32), ("diag", [P, NB], F32),
                                      ("end_col", [P, 1], F32), ("after", [P, TT // 4], F32)):
                    t[n_] = inner.enter_context(nc.sbuf_tensor(f"sort_{n_}", shape, dt))
                base_ps = inner.enter_context(nc.psum_tensor("base_ps", [P, 2, 512], F32))
                m = {n_: signals.new(f"sort_{n_}") for n_ in
                     ("steps", "counted", "prefixed", "compared", "tiled", "turn", "iota_t")}
                m["n"] = Count()
                fill_order(nc, "order_a", order_a, pad_a)
                fill_order(nc, "order_b", order_b, pad_b)

                with ExitStack() as first:
                    w_all, load_w, w_loaded = typed_weights(nc, first, "w0", L0_gnn_W[0])
                    with nc.Block() as block:
                        pe_y, act_y, sp_y = typed_rows(nc, block, first, "y0", c, h, w_all, typed_table)

                        @block.gpsimd
                        def _(pool):
                            pool.iota(t["iota_t"], [[1, TT]], base=0, channel_multiplier=0,
                                      allow_small_or_imprecise_dtypes=True).then_inc(m["iota_t"], 1)

                        @block.sync
                        def _(sp):
                            load_w(sp)
                            sp_y(sp)

                        @block.scalar
                        def _(act):
                            act_y(act)

                        @block.tensor
                        def _(pe):
                            find_places_pe(pe, 0, c, t, base_ps, m, between=lambda pe: pe_y(pe, w_loaded))

                        @block.vector
                        def _(dve):
                            dve.memset(t["ones_e"], 1.0).then_inc(m["steps"], m["n"].up())
                            dve.wait_ge(m["iota_t"], 1)
                            find_places(nc, dve, 0, c, t, key_a, place_a, tiles_a, base_ps, m)

                with ExitStack() as moving:
                    act_s, pool_s = scatter_records(nc, moving, "move_a", rec_a, place_a.bitcast(I32), order_a)
                    with nc.Block() as block:
                        @block.scalar
                        def _(act):
                            act_s(act)

                        @block.gpsimd
                        def _(pool):
                            pool_s(pool)

                        @block.tensor
                        def _(pe):
                            find_places_pe(pe, 1, c, t, base_ps, m)

                        @block.vector
                        def _(dve):
                            find_places(nc, dve, 1, c, t, key_b, place_b, tiles_b, base_ps, m)
                load_order(nc, "load_a", order_a, rec_a)

            with ExitStack() as moving:
                act_s, pool_s = scatter_records(nc, moving, "move_b", rec_b, place_b.bitcast(I32), order_b)
                edge_pass(nc, "count", "count", c, rec_a, 0, 2, acc, R, acc_row=tiles_a[32:33, :],
                          beside={"act": act_s, "pool": pool_s})
            load_order(nc, "load_b", order_b, rec_b)

        signals.clear()
        in_a_row(nc, "counts", [
            ("v", lambda: v.tensor_reduce(inv_deg[:, :], acc3[:, :, 0:R], AX.X, ALU.add)),
            ("v", lambda: v.tensor_scalar(s_src[:, :], inv_deg[:, :], 1.0, None, ALU.max)),
            ("a", lambda: a.activation(s_src[:, :], s_src[:, :], ACT.Sqrt)),
            ("v", lambda: v.tensor_scalar(inv_deg[:, :], inv_deg[:, :], 0.0, None, ALU.is_gt)),
            ("v", lambda: v.reciprocal(s_src[:, :], s_src[:, :])),
            ("v", lambda: v.tensor_tensor(inv_deg[:, :], inv_deg[:, :], s_src[:, :], ALU.mult)),
            ("v", lambda: v.memset(tab[:, :], 0.0)),
            ("v", lambda: v.tensor_scalar(acc3[:, :, 0:R], acc3[:, :, 0:R], 1.0, None, ALU.max)),
            ("v", lambda: v.reciprocal(tab3[:, :, 0:R], acc3[:, :, 0:R])),
        ])

        def relational_end(l, x_tile=None):
            with ExitStack() as inner:
                part = [inner.enter_context(nc.sbuf_tensor(f"part{l}_{s}", [P, 2, 2 * D], F32)) for s in range(2)]
                K = 5 if x_tile is not None else 4

                def consume(dve, s, res, used):
                    b = part[s.slot]
                    dve.tensor_tensor(b[:, :, :], res, biases[l][:, :].unsqueeze(1).broadcast_to([P, 2, 2 * D]),
                                      ALU.add).then_inc(used, 1)
                    dve.wait_ge(used, s.g * K + 1)
                    sums = acc[:, bass.ds(s.g * (2 * WIDE), 2 * WIDE)].rearrange("p (b w) -> p b w", w=WIDE)[:, :, 0:D]
                    dve.tensor_tensor(b[:, :, 0:D], b[:, :, 0:D], sums, ALU.add).then_inc(used, 1)
                    dve.wait_ge(used, s.g * K + 2)
                    dve.tensor_scalar(b[:, :, :], b[:, :, :], 0.0, None, ALU.max).then_inc(used, 1)
                    dve.wait_ge(used, s.g * K + 3)
                    to = (h if x_tile is None else x_tile)[:, bass.ds(s.g * (2 * D), 2 * D)].rearrange("p (b d) -> p b d", d=D)
                    if x_tile is None:
                        dve.tensor_tensor(to, b[:, :, 0:D], b[:, :, D:2 * D], ALU.add).then_inc(used, 1)
                    else:
                        dve.tensor_tensor(to, to, b[:, :, 0:D], ALU.add).then_inc(used, 1)
                        dve.wait_ge(used, s.g * K + 4)
                        dve.tensor_tensor(to, to, b[:, :, D:2 * D], ALU.add).then_inc(used, 1)
                times_weights(nc, f"rel{l}", c, h, root_res[l], 2 * D, consume, K)

        row_a, row_b = tiles_a[32:33, :], tiles_b[32:33, :]
        signals.clear()
        edge_pass(nc, "typed0", "typed", c, rec_a, 0, 2, acc, D, table=typed_table, tw=D, own=tab, ow=R,
                  own_row=row_a, acc_row=row_a)
        relational_end(0)
        with ExitStack() as second:
            w_all, load_w, w_loaded = typed_weights(nc, second, "w1", L0_gnn_W[1])
            with nc.Block() as block:
                pe_y, act_y, sp_y = typed_rows(nc, block, second, "y1", c, h, w_all, typed_table)

                @block.sync
                def _(sp):
                    load_w(sp)
                    sp_y(sp)

                @block.scalar
                def _(act):
                    act_y(act)

                @block.tensor
                def _(pe):
                    pe_y(pe, w_loaded)
        edge_pass(nc, "typed1", "typed_again", c, rec_a, 0, 2, acc, D, table=typed_table, tw=D, acc_row=row_a)
        signals.clear()
        xt = sb("xt", [P, NB * D])
        x3 = xt[:, :].rearrange("p (b d) -> p b d", d=D)
        with ExitStack() as inner:
            cleared, loaded = (signals.new(n) for n in ("x_cleared", "x_loaded"))
            with nc.Block() as block:
                @block.vector
                def _(dve):
                    dve.memset(xt[:, (NB - 1) * D:NB * D], 0.0).then_inc(cleared, 1)

                @block.sync
                def _(sp):
                    sp.wait_ge(cleared, 1)
                    sp.dma_start(x3[:, 0:NB - 1, :], x[0:(NB - 1) * P, :].rearrange("(b p) d -> p b d", p=P)).then_inc(loaded, 16)
                    sp.dma_start(x3[0:NLAST, NB - 1, :], x[(NB - 1) * P:N, :]).then_inc(loaded, 16)
                    sp.wait_ge(loaded, 32)
        relational_end(1, xt)

        def rows(ap, n):
            return ap.unsqueeze(1).broadcast_to([P, NB, n])

        def cols(ap, n):
            return ap.unsqueeze(2).broadcast_to([P, NB, n])

        signals.clear()
        normalize(nc, "norm1", x3, h3, acc3)
        with ExitStack() as inner:
            def consume(dve, s, res, used):
                to = tab[:, bass.ds(s.g * (2 * WIDE), 2 * WIDE)].rearrange("p (b w) -> p b w", w=WIDE)[:, :, 0:D]
                dve.tensor_tensor(to, res, rows_of["b_cos"][:, :].unsqueeze(1).broadcast_to([P, 2, D]), ALU.add).then_inc(used, 1)
            times_weights(nc, "cos", c, h, w_cos, D, consume, 1)
        in_a_row(nc, "norms", [
            ("v", lambda: v.tensor_tensor(acc3[:, :, 0:D], tab3[:, :, 0:D], tab3[:, :, 0:D], ALU.mult)),
            ("v", lambda: v.tensor_reduce(s_src[:, :], acc3[:, :, 0:D], AX.X, ALU.add)),
            ("v", lambda: v.tensor_scalar(s_src[:, :], s_src[:, :], 1e-30, None, ALU.max)),
            ("a", lambda: a.activation(tab3[:, :, D], s_src[:, :], ACT.Sqrt)),
        ])
        store_table(nc, "cos_table", tab3, node_table, WIDE)
        edge_pass(nc, "cosine", "cosine", c, rec_b, 0, 1, acc, D, table=node_table, tw=WIDE, own=tab, ow=R,
                  own_row=row_b, acc_row=row_b)
        in_a_row(nc, "cos_end", [
            ("v", lambda: v.tensor_scalar(tab3[:, :, 0:D], tab3[:, :, 0:D], coeff[:, 2:3], None, ALU.mult)),
            ("v", lambda: v.tensor_tensor(acc3[:, :, 0:D], acc3[:, :, 0:D], tab3[:, :, 0:D], ALU.add)),
            ("v", lambda: v.tensor_scalar(acc3[:, :, 0:D], acc3[:, :, 0:D], coeff[:, 3:4], None, ALU.mult)),
            ("v", lambda: v.tensor_tensor(x3, x3, acc3[:, :, 0:D], ALU.add)),
        ])

        signals.clear()
        normalize(nc, "norm2", x3, h3, acc3)
        in_a_row(nc, "att_begin", [
            ("v", lambda: v.memset(tab3[:, :, D:D + 1], 1.0)),
            ("v", lambda: v.tensor_tensor(tab3[:, :, 0:D], h3, rows(rows_of["w_att"][:, :], D), ALU.mult)),
            ("v", lambda: v.tensor_tensor(h3, tab3[:, :, 0:D], rows(rows_of["a_att"][:, 0:D], D), ALU.mult)),
            ("v", lambda: v.tensor_reduce(s_src[:, :], h3, AX.X, ALU.add)),
            ("v", lambda: v.tensor_tensor(h3, tab3[:, :, 0:D], rows(rows_of["a_att"][:, D:2 * D], D), ALU.mult)),
            ("v", lambda: v.tensor_reduce(tab3[:, :, D + 1], h3, AX.X, ALU.add)),
        ])
        store_table(nc, "att_table", tab3, node_table, WIDE)
        edge_pass(nc, "attention", "attention", c, rec_b, 0, 1, acc, D + 1, table=node_table, tw=WIDE, own=s_src, ow=1,
                  own_row=tiles_b[0:1, :], acc_row=row_b)
        in_a_row(nc, "att_end", [
            ("v", lambda: v.tensor_scalar(acc3[:, :, D], acc3[:, :, D], 1e-37, None, ALU.max)),
            ("v", lambda: v.reciprocal(s_src[:, :], acc3[:, :, D])),
            ("v", lambda: v.tensor_tensor(acc3[:, :, 0:D], acc3[:, :, 0:D], cols(s_src[:, :], D), ALU.mult)),
            ("v", lambda: v.tensor_scalar(h3, acc3[:, :, 0:D], 0.0, None, ALU.min)),
            ("a", lambda: a.activation(h3, h3, ACT.Exp)),
            ("v", lambda: v.tensor_scalar(h3, h3, -1.0, None, ALU.add)),
            ("v", lambda: v.scalar_tensor_tensor(out=h3, in0=acc3[:, :, 0:D], scalar=0.0, in1=h3, op0=ALU.max, op1=ALU.add)),
            ("v", lambda: v.tensor_tensor(x3, x3, h3, ALU.add)),
        ])

        signals.clear()
        normalize(nc, "norm3", x3, h3, acc3)
        in_a_row(nc, "prop_begin", [
            ("v", lambda: v.tensor_tensor(tab3[:, :, 0:D], h3, cols(inv_deg[:, :], D), ALU.mult)),
        ])
        store_table(nc, "prop_table", tab3, node_table, WIDE)
        edge_pass(nc, "prop0", "plain", c, rec_a, 1, 2, acc, D, table=node_table, tw=WIDE, acc_row=row_a)
        signals.clear()
        in_a_row(nc, "prop_mid", [
            ("v", lambda: v.tensor_tensor(acc3[:, :, 0:D], acc3[:, :, 0:D], cols(inv_deg[:, :], D), ALU.mult)),
            ("v", lambda: v.tensor_tensor(h3, h3, acc3[:, :, 0:D], ALU.add)),
            ("v", lambda: v.tensor_tensor(tab3[:, :, 0:D], acc3[:, :, 0:D], cols(inv_deg[:, :], D), ALU.mult)),
        ])
        store_table(nc, "prop_table2", tab3, node_table, WIDE)
        edge_pass(nc, "prop1", "plain", c, rec_a, 1, 2, acc, D, table=node_table, tw=WIDE, acc_row=row_a)
        in_a_row(nc, "prop_end", [
            ("v", lambda: v.tensor_tensor(acc3[:, :, 0:D], acc3[:, :, 0:D], cols(inv_deg[:, :], D), ALU.mult)),
            ("v", lambda: v.tensor_tensor(h3, h3, acc3[:, :, 0:D], ALU.add)),
            ("v", lambda: v.tensor_scalar(h3, h3, 0.3, None, ALU.mult)),
            ("v", lambda: v.tensor_tensor(x3, x3, rows(rows_of["b_out"][:, :], D), ALU.add)),
        ])

        def consume(dve, s, res, used):
            to = xt[:, bass.ds(s.g * (2 * D), 2 * D)].rearrange("p (b d) -> p b d", d=D)
            dve.tensor_tensor(to, to, res, ALU.add).then_inc(used, 1)
        times_weights(nc, "prop", c, h, w_out, D, consume, 1)
        with ExitStack() as inner:
            stored = signals.new("out_stored")
            with nc.Block() as block:
                @block.sync
                def _(sp):
                    sp.dma_start(out[0:(NB - 1) * P, :].rearrange("(b p) d -> p b d", p=P), x3[:, 0:NB - 1, :]).then_inc(stored, 16)
                    sp.dma_start(out[(NB - 1) * P:N, :], x3[0:NLAST, NB - 1, :]).then_inc(stored, 16)
                    sp.wait_ge(stored, 32)


_INS = ["x", "src", "dst", "edge_type_65", "edge_weight", "edge_weight_n2", "L0_gnn_W", "L0_gnn_root", "L0_gnn_bias",
        "L0_gnn_res_W", "L0_gnn_res_b", "L1_gnn_W", "L1_gnn_b", "L1_gnn_deg_coeff", "L1_gnn_coeff_param",
        "L1_gnn_scale_param", "L2_gnn_W", "L2_gnn_a", "L3_gnn_W", "L3_gnn_b"]


def kernel(**inputs):
    import numpy as _np
    import concourse.bacc as _bacc
    from concourse import mybir as _mybir
    from concourse.bass_utils import run_bass_kernel_spmd as _run

    nc = _bacc.Bacc("TRN2", target_bir_lowering=False, num_devices=1)
    arrays, args = {}, []
    for name in _INS:
        a = _np.ascontiguousarray(inputs[name])
        arrays[f"in_{name}_dram"] = a
        args.append(nc.dram_tensor(f"in_{name}_dram", a.shape, _mybir.dt.from_np(a.dtype), kind="ExternalInput").ap())
    args.append(nc.dram_tensor("out_dram", (N, D), _mybir.dt.float32, kind="ExternalOutput").ap())
    gnn_kernel(nc, *args)
    r = _run(nc, [arrays], core_ids=[0])
    return r.results[0]["out_dram"]
```
